# Optimizing a Trainium2 kernel written in Bass

```python
import numpy as np
import jax
import jax.numpy as jnp

def _softmax(x, axis=-1):
    return jax.nn.softmax(x, axis=axis)

def _gelu(x):
    return jax.nn.gelu(x, approximate=True)

def _silu(x):
    return jax.nn.silu(x)

def _sigmoid(x):
    return jax.nn.sigmoid(x)

def _layernorm(x, axis=-1, eps=1e-05):
    m = jnp.mean(x, axis=axis, keepdims=True)
    v = jnp.var(x, axis=axis, keepdims=True)
    return (x - m) / jnp.sqrt(v + eps)

def _scatter_add(tgt, idx, src, axis=0):
    return tgt.at[idx].add(src)

def _segment_sum(src, seg, n):
    return jax.ops.segment_sum(src, seg, n)
kernel_name = 'mk_rec_standalone_d1_rec_r8_721921'

def setup_inputs(seed: int=0):
    np.random.seed(seed)
    _w = jnp.asarray

    def _rec_inputs():
        import jax
        import jax.numpy as jnp
        _rk = jax.random.key(seed)
        r_inputs = -0.000886322 + 1.00077 * jax.random.normal(jax.random.fold_in(_rk, 1), (512, 26, 32), jnp.float32)
        return r_inputs
    r_inputs = _rec_inputs()

    def _L0_rec_setup():
        import jax, jax.numpy as jnp
        import numpy as np
        M_FIELDS = 26
        H1 = 128
        H2 = 128
        BATCH = 256
        EMB_K = 32

        def _cin_layer(x_prev, x0, W, b):
            return jnp.einsum('bik,bjk,hij->bhk', x_prev, x0, W) + b[None, :, None]
        key = jax.random.key(seed)
        k0, k1, k2, k3, k4 = jax.random.split(key, 5)
        inputs = jax.random.normal(k0, (BATCH, M_FIELDS, EMB_K), dtype=jnp.float32)
        W1 = jax.random.normal(k1, (H1, M_FIELDS, M_FIELDS), dtype=jnp.float32) * 0.05
        b1 = jax.random.normal(k2, (H1,), dtype=jnp.float32) * 0.05
        W2 = jax.random.normal(k3, (H2, H1, M_FIELDS), dtype=jnp.float32) * 0.05
        b2 = jax.random.normal(k4, (H2,), dtype=jnp.float32) * 0.05
        return {'inputs': inputs, 'W1': W1, 'b1': b1, 'W2': W2, 'b2': b2}
    _L0_rec_all = _L0_rec_setup()
    _L0_rec_in = {k: v for k, v in _L0_rec_all.items() if k in ('W1', 'b1', 'W2', 'b2')}
    del _L0_rec_all
    return {'r_inputs': r_inputs, 'L0_rec_W1': _L0_rec_in['W1'], 'L0_rec_b1': _L0_rec_in['b1'], 'L0_rec_W2': _L0_rec_in['W2'], 'L0_rec_b2': _L0_rec_in['b2']}

def reference(r_inputs, L0_rec_W1, L0_rec_b1, L0_rec_W2, L0_rec_b2):
    import jax
    import jax.numpy as jnp

    def _L0_rec_ref(inputs, W1, b1, W2, b2):
        import jax, jax.numpy as jnp
        import numpy as np
        M_FIELDS = 26
        H1 = 128
        H2 = 128
        BATCH = 256
        EMB_K = 32

        def _cin_layer(x_prev, x0, W, b):
            return jnp.einsum('bik,bjk,hij->bhk', x_prev, x0, W) + b[None, :, None]
        x1 = _cin_layer(inputs, inputs, W1, b1)
        x2 = _cin_layer(x1, inputs, W2, b2)
        res = jnp.concatenate([x1, x2], axis=1)
        return jnp.sum(res, axis=-1)
    y = _L0_rec_ref(r_inputs, L0_rec_W1, L0_rec_b1, L0_rec_W2, L0_rec_b2)
    return y

_drawn_inputs = setup_inputs


def setup_inputs(seed=0):
    import zlib

    import numpy as np

    out = dict(_drawn_inputs(seed))
    spreads = {}
    factors = {}
    for name, (base, spread) in spreads.items():
        noise = np.random.default_rng([zlib.crc32(name.encode()), seed]).standard_normal(out[name].shape)
        drawn = base * np.exp(spread * noise) if base else spread * noise
        out[name] = jnp.asarray(drawn.astype(out[name].dtype))
    for name, factor in factors.items():
        out[name] = (out[name] * factor).astype(out[name].dtype)
    return out
```

```python
from contextlib import ExitStack

import numpy as np

import concourse.bass as bass
from concourse import mybir

F32 = mybir.dt.float32
ACT = mybir.ActivationFunctionType
ALU = mybir.AluOpType

BATCH, M, K = 512, 26, 32
H = 128
MC = M + 1
BL = 128 // K
GROUPS = BATCH // BL
GB = 16
BLOCKS = GROUPS // GB
BANK = 512
RING = 7


class Chunk:

    def __init__(self, lo, hi, col, unit, cunit):
        self.lo, self.hi = lo, hi
        self.col = col
        self.const = 1 if lo == 0 else 0
        self.diag = self.const
        self.run = {}
        at = self.diag + hi - lo
        for b in range(lo, hi):
            self.run[b] = at
            at += b
        self.size = at
        self.thirds = MC - lo
        self.unit = unit
        self.cunit = cunit
        self.per_bank = max(n for n in (1, 2, 4, 8, 16) if n * BL * self.thirds <= BANK)
        self.fills = GB // self.per_bank


def plan_chunks():
    chunks, col, unit, cunit = [], 0, 0, 0
    for lo, hi in ((0, 15), (15, 21), (21, 26)):
        c = Chunk(lo, hi, col, unit, cunit)
        assert c.size <= 128
        chunks.append(c)
        col, unit, cunit = col + c.size, unit + c.thirds, cunit + c.thirds - 1
    return chunks, col, unit, cunit


CHUNKS, PAIRS, UNITS, CUNITS = plan_chunks()
FILLS = sum(c.fills for c in CHUNKS)
L0 = CHUNKS[1].lo
NL = M - L0
JD = CHUNKS[2].lo
assert FILLS == RING


def build(nc, x_cols, w_pairs, w1_t, w2_t, b2, eye, out_t):
    ctx = ExitStack()
    with ctx:
        def sb(name, shape):
            return ctx.enter_context(nc.sbuf_tensor(name, shape, F32))

        def sem(name):
            return ctx.enter_context(nc.semaphore(name))

        x_dense = sb("x_dense", [128, GROUPS, MC])
        x_diag = sb("x_diag", [128, 2, BL, GB, MC])
        slot0 = sb("slot0", [128, GB * PAIRS])
        slot1 = sb("slot1", [128, max(GB * PAIRS, JD * NL * M)])
        prods = [s[:, 0:GB * PAIRS].rearrange("p (g n) -> p g n", n=PAIRS) for s in (slot0, slot1)]
        w_raw = slot1[:, 0:2 * (PAIRS + NL * M)].rearrange("p (a n) -> p a n", a=2)
        d_sb = slot1[:, 0:JD * NL * M].rearrange("p (j l i) -> p j l i", l=NL, i=M)
        res = slot0[:, 0:2 * BATCH].rearrange("p (a b) -> p a b", a=2)
        moments = sb("moments", [128, UNITS, BATCH])
        w_sum = sb("w_sum", [128, PAIRS + NL * M])
        u_t_raw = sb("u_t_raw", [128, 2, len(CHUNKS), H])
        u_t = sb("u_t", [128, len(CHUNKS), H])
        w2s = sb("w2s", [128, M, H])
        ident = sb("ident", [128, H])
        b2_raw = sb("b2_raw", [128, 1])
        b2_k = sb("b2_k", [128, 1])
        half = BATCH // 2
        moved = [moments[:, NL * n:NL * n + (NL if n < 2 else M - c.lo), half:half + c.size]
                 for n, c in enumerate(CHUNKS)]
        coef = sb("coef", [128, CUNITS, H])
        ps = ctx.enter_context(nc.psum_tensor("ps", [128, 8, BANK], F32))

        w_loaded = sem("w_loaded")
        w2_loaded = sem("w2_loaded")
        small_loaded = sem("small_loaded")
        x_first = sem("x_first")
        x_rest = sem("x_rest")
        diag_zeroed = sem("diag_zeroed")
        diag_loaded = [sem("diag_loaded0"), sem("diag_loaded1")]
        ones_set = sem("ones_set")
        moved_zeroed = sem("moved_zeroed")
        w_summed = sem("w_summed")
        moved_ready = sem("moved_ready")
        prods_ready = sem("prods_ready")
        weights_filled = sem("weights_filled")
        filled = sem("filled")
        evacuated = sem("evacuated")
        first_sum = sem("first_sum")
        second_sum = sem("second_sum")
        b2_ready = sem("b2_ready")
        res_ready = sem("res_ready")
        stored = sem("stored")

        D_PER_BANK = BANK // ((M - JD) * M)
        d_fills = [[j] for j in range(L0)] + [list(range(j, min(j + D_PER_BANK, JD)))
                                              for j in range(L0, JD, D_PER_BANK)]
        c_fills = [(n, s, min(s + 4, c.thirds - 1)) for n, c in enumerate(CHUNKS)
                   for s in range(0, c.thirds - 1, 4)]
        D_BASE = 0
        T0_BASE = D_BASE + len(d_fills)
        C_BASE = T0_BASE + FILLS
        T_BASE = C_BASE + len(c_fills) - FILLS

        def bank(n):
            return ps[:, n % RING, :]

        def diagonal(a0, a1, l0):
            return bass.AP(tensor=slot1, offset=a0 * (NL * M + 1) + l0 * M,
                           ap=[[slot1.shape[1], 128], [NL * M + 1, a1 - a0], [M, NL - l0]])

        def d_width(j):
            return (NL if j < L0 else M - JD) * M

        def x_rows(bl, t):
            return x_cols[K * bl:K * bl + K, bass.ds(t * (GB * MC), GB * MC)]

        block = ctx.enter_context(nc.Block())

        @block.sync
        def _(sp):
            def load_diag(t, slot):
                for bl in range(BL):
                    sp.dma_start(x_diag[K * bl:K * bl + K, slot, bl].rearrange("p g m -> p (g m)"),
                                 x_rows(bl, t)).then_inc(diag_loaded[slot], 16)

            flat = x_dense[:, :, :].rearrange("p g m -> p (g m)")
            sp.dma_start(slot1[:, 0:2 * (PAIRS + NL * M)], w_pairs).then_inc(w_loaded, 16)
            sp.dma_start(flat[:, 0:GB * MC], x_cols[:, 0:GB * MC]).then_inc(x_first, 16)
            for slot in range(2):
                sp.wait_ge(diag_zeroed, slot + 1)
                load_diag(slot, slot)
            sp.dma_start(flat[:, GB * MC:], x_cols[:, GB * MC:]).then_inc(x_rest, 16)
            with sp.Fori(1, BLOCKS // 2) as i:
                for slot in range(2):
                    sp.wait_ge(filled, i * (2 * FILLS) + (slot - 1) * FILLS)
                    load_diag(2 * i + slot, slot)
            for n in range(2):
                sp.wait_ge(res_ready, n + 1)
                sp.dma_start(out_t[n], res[:, n, :]).then_inc(stored, 16)
            sp.wait_ge(stored, 32)

        @block.gpsimd
        def _(pool):
            for slot in range(2):
                nc.gpsimd.memset(x_diag[:, slot], 0.0).then_inc(diag_zeroed, 1)
            for n in range(len(CHUNKS)):
                nc.gpsimd.memset(moved[n][:, :, :], 0.0).then_inc(moved_zeroed, 1)

        @block.vector
        def _(dve):
            def pair_products(t, slot):
                x = x_dense[:, bass.ds(t * GB, GB), :]
                done = 0
                for n, c in enumerate(CHUNKS):
                    done += c.fills
                    if not isinstance(t, int):
                        dve.wait_ge(filled, t * FILLS + (done - 2 * FILLS))
                    out = prods[slot][:, :, c.col:c.col + c.size]
                    w = c.hi - c.lo
                    last = nc.vector.tensor_tensor(out[:, :, c.diag:c.diag + w], x[:, :, c.lo:c.hi],
                                                   x[:, :, c.lo:c.hi], ALU.mult)
                    for b in range(max(c.lo, 1), c.hi):
                        last = nc.vector.tensor_tensor(
                            out[:, :, c.run[b]:c.run[b] + b], x[:, :, 0:b],
                            x[:, :, b:b + 1].to_broadcast([128, GB, b]), ALU.mult)
                    last.then_inc(prods_ready, 1)

            nc.vector.memset(prods[0][:, :, 0:1], 1.0).then_inc(ones_set, 1)
            dve.wait_ge(w_loaded, 16)
            nc.vector.tensor_tensor(w_sum[:, :], w_raw[:, 0, :], w_raw[:, 1, :], ALU.add).then_inc(w_summed, 1)
            dve.wait_ge(x_first, 16)
            pair_products(0, 0)
            dve.wait_ge(small_loaded, 48)
            nc.vector.tensor_tensor(u_t[:, :, :], u_t_raw[:, 0], u_t_raw[:, 1], ALU.add).then_inc(w_summed, 1)
            nc.vector.tensor_scalar(b2_k[:, :], b2_raw[:, :], float(K), None, ALU.mult).then_inc(b2_ready, 1)

            dve.wait_ge(evacuated, T0_BASE)
            dve.wait_ge(moved_zeroed, len(CHUNKS))
            c0, c1, c2 = CHUNKS
            o0, o1, o2 = moved
            late = JD - L0
            nc.vector.tensor_copy(
                o0[:, :, c0.diag:c0.diag + c0.hi].rearrange("p l a -> p a l"),
                diagonal(0, c0.hi, 0))
            nc.vector.tensor_copy(
                o1[:, late:, c1.diag:c1.diag + c1.hi - c1.lo].rearrange("p l a -> p a l"),
                diagonal(c1.lo, c1.hi, late))
            for b in range(1, c0.hi):
                nc.vector.tensor_tensor(o0[:, :, c0.run[b]:c0.run[b] + b], d_sb[:, b, :, 0:b],
                                        d_sb[:, 0:b, :, b].rearrange("p a l -> p l a"), ALU.add)
            for b in range(c1.lo, c1.hi):
                nc.vector.tensor_tensor(o1[:, late:, c1.run[b]:c1.run[b] + b], d_sb[:, b, late:, 0:b],
                                        d_sb[:, 0:b, late:, b].rearrange("p a l -> p l a"), ALU.add)
                nc.vector.tensor_copy(o1[:, b - L0:late, c1.run[b]:c1.run[b] + L0],
                                      d_sb[:, 0:L0, b - L0:late, b].rearrange("p a l -> p l a"))
            for b in range(c2.lo, c2.hi):
                last = nc.vector.tensor_copy(o2[:, b - c2.lo:, c2.run[b]:c2.run[b] + JD],
                                             d_sb[:, 0:JD, b - L0:, b].rearrange("p a l -> p l a"))
            last.then_inc(moved_ready, 1)
            dve.wait_ge(moved_ready, 1)
            nc.vector.memset(prods[1][:, :, 0:1], 1.0).then_inc(ones_set, 1)
            dve.wait_ge(x_rest, 16)
            pair_products(1, 1)
            with dve.Fori(1, BLOCKS // 2) as i:
                for slot in range(2):
                    pair_products(2 * i + slot, slot)

        @block.tensor
        def _(pe):
            def bank_free(n):
                if not isinstance(n, int) or n >= RING:
                    pe.wait_ge(evacuated, n + (1 - RING))

            def moments_of(slot, first_bank, base, ready, diag_count):
                pe.wait_ge(diag_loaded[slot], diag_count)
                f = 0
                for n, c in enumerate(CHUNKS):
                    pe.wait_ge(prods_ready, ready + n)
                    width = BL * c.thirds
                    for q in range(c.fills):
                        bank_free(base + f)
                        out = bank(first_bank + f)
                        for g in range(c.per_bank):
                            gg = q * c.per_bank + g
                            last = nc.tensor.matmul(
                                out[0:c.size, g * width:(g + 1) * width],
                                prods[slot][:, gg, c.col:c.col + c.size],
                                x_diag[:, slot, :, gg, c.lo:MC], start=True, stop=True)
                        last.then_inc(filled, 1)
                        f += 1

            pe.wait_ge(w_summed, 1)
            pe.wait_ge(w2_loaded, 16)
            for n, js in enumerate(d_fills):
                bank_free(D_BASE + n)
                for s, j in enumerate(js):
                    w = d_width(j)
                    last = nc.tensor.matmul(bank(D_BASE + n)[:, s * w:(s + 1) * w], w2s[:, j, :],
                                            w_sum[:, PAIRS + NL * M - w:], start=True, stop=True)
                last.then_inc(weights_filled, 1)

            moments_of(0, T0_BASE, T0_BASE, 1, 16 * BL)

            pe.wait_ge(small_loaded, 48)
            pe.wait_ge(moved_ready, 1)
            for m, (n, s0, s1) in enumerate(c_fills):
                c = CHUNKS[n]
                bank_free(C_BASE + m)
                out = bank(C_BASE + m)
                slots = [s for s in range(s0, s1) if c.lo + s >= L0]
                last = nc.tensor.matmul(out[0:c.size, 0:(s1 - s0) * H], w_sum[:, c.col:c.col + c.size],
                                        w2s[:, c.lo + s0:c.lo + s1, :], start=True, stop=not slots)
                for s in slots:
                    l = c.lo + s - (L0 if n < 2 else c.lo)
                    last = nc.tensor.matmul(out[0:c.size, (s - s0) * H:(s - s0 + 1) * H],
                                            moved[n][:, l, :], ident[:, :], start=False,
                                            stop=s == slots[-1])
                last.then_inc(weights_filled, 1)

            moments_of(1, T_BASE, T_BASE + FILLS, 4, 16 * BL)
            with pe.Fori(1, BLOCKS // 2) as i:
                for slot in range(2):
                    moments_of(slot, T_BASE, T_BASE + FILLS * slot + i * (2 * FILLS), 3 * slot + 1 + i * 6,
                               (i + 1) * (16 * BL))

            pe.wait_ge(w_summed, 2)
            pe.wait_ge(evacuated, T_BASE + FILLS * BLOCKS)
            for n, c in enumerate(CHUNKS):
                last = nc.tensor.matmul(ps[:, 0, :], u_t[0:c.size, n, :],
                                        moments[0:c.size, c.unit + c.thirds - 1, :],
                                        start=n == 0, stop=n == len(CHUNKS) - 1)
            last.then_inc(first_sum, 1)
            for n, c in enumerate(CHUNKS):
                for s in range(c.thirds - 1):
                    last = nc.tensor.matmul(ps[:, RING, :], coef[0:c.size, c.cunit + s, :],
                                            moments[0:c.size, c.unit + s, :],
                                            start=n == 0 and s == 0,
                                            stop=n == len(CHUNKS) - 1 and s == c.thirds - 2)
            last.then_inc(second_sum, 1)

        @block.scalar
        def _(act):
            act.dma_start(w2s[:, :, :].rearrange("p j h -> p (j h)"), w2_t).then_inc(w2_loaded, 16)
            act.dma_start(u_t_raw[:, :, :, :].rearrange("p a n h -> p (a n h)"), w1_t).then_inc(small_loaded, 16)
            act.dma_start(ident[:, :], eye).then_inc(small_loaded, 16)
            act.dma_start(b2_raw[:, :], b2).then_inc(small_loaded, 16)

            def keep_moments(t, first_bank):
                f = 0
                for c in CHUNKS:
                    nb = c.per_bank * BL
                    for q in range(c.fills):
                        act.wait_ge(filled, t * FILLS + (f + 1))
                        src = bank(first_bank + f)[0:c.size, 0:nb * c.thirds]
                        nc.scalar.activation(
                            moments[0:c.size, c.unit:c.unit + c.thirds, bass.ds(t * (GB * BL) + q * nb, nb)],
                            src.rearrange("p (b m) -> p m b", m=c.thirds), ACT.Copy).then_inc(evacuated, 1)
                        f += 1

            for n, js in enumerate(d_fills):
                act.wait_ge(weights_filled, n + 1)
                w = d_width(js[0])
                nc.scalar.activation(
                    d_sb[:, js[0]:js[-1] + 1, NL - w // M:, :].rearrange("p j l i -> p j (l i)"),
                    bank(D_BASE + n)[:, 0:w * len(js)].rearrange("p (j w) -> p j w", w=w),
                    ACT.Copy).then_inc(evacuated, 1)
            keep_moments(0, T0_BASE)
            for m, (n, s0, s1) in enumerate(c_fills):
                c = CHUNKS[n]
                act.wait_ge(weights_filled, len(d_fills) + m + 1)
                nc.scalar.activation(
                    coef[0:c.size, c.cunit + s0:c.cunit + s1, :].rearrange("p s h -> p (s h)"),
                    bank(C_BASE + m)[0:c.size, 0:(s1 - s0) * H], ACT.Copy).then_inc(evacuated, 1)
            keep_moments(1, T_BASE)
            with act.Fori(1, BLOCKS // 2) as i:
                for slot in range(2):
                    keep_moments(2 * i + slot, T_BASE)
            act.wait_ge(first_sum, 1)
            nc.scalar.activation(res[:, 0, :], ps[:, 0, :], ACT.Copy).then_inc(res_ready, 1)
            act.wait_ge(b2_ready, 1)
            act.wait_ge(second_sum, 1)
            nc.scalar.activation(res[:, 1, :], ps[:, RING, :], ACT.Identity,
                                 bias=b2_k[:, 0:1]).then_inc(res_ready, 1)


def kernel(r_inputs, L0_rec_W1, L0_rec_b1, L0_rec_W2, L0_rec_b2):
    import concourse.bacc as bacc
    from concourse.bass_utils import run_bass_kernel_spmd

    x, w1, b1, w2, b2 = (np.asarray(a) for a in (r_inputs, L0_rec_W1, L0_rec_b1, L0_rec_W2, L0_rec_b2))
    x_cols = np.ones((BL, K, GROUPS, MC), np.float32)
    x_cols[..., :M] = x.reshape(GROUPS, BL, M, K).transpose(1, 3, 0, 2)
    pairs = np.zeros((2, H, PAIRS), np.float32)
    for c in CHUNKS:
        if c.const:
            pairs[0, :, c.col] = b1
        for a in range(c.lo, c.hi):
            pairs[0, :, c.col + c.diag + a - c.lo] = w1[:, a, a]
            pairs[0, :, c.col + c.run[a]:c.col + c.run[a] + a] = w1[:, :a, a]
            pairs[1, :, c.col + c.run[a]:c.col + c.run[a] + a] = w1[:, a, :a]
    rows = np.zeros((2, H, NL, M), np.float32)
    rows[0] = w1[:, L0:, :]
    rows[1] = w1[:, :, L0:].transpose(0, 2, 1)
    for l in range(L0, M):
        rows[1, :, l - L0, l] = 0.0
    w_pairs = np.concatenate([pairs, rows.reshape(2, H, NL * M)], axis=2).transpose(1, 0, 2)
    w1_t = np.zeros((128, 2, len(CHUNKS), H), np.float32)
    for n, c in enumerate(CHUNKS):
        w1_t[:c.size, :, n, :] = pairs[:, :, c.col:c.col + c.size].transpose(2, 0, 1)
    arrays = {
        "x_cols": x_cols.reshape(128, GROUPS * MC),
        "w_pairs": w_pairs.reshape(H, -1),
        "w1_t": w1_t.reshape(128, -1),
        "w2_t": w2.transpose(1, 2, 0).reshape(H, M * H),
        "b2": b2.reshape(H, 1),
        "eye": np.eye(H, dtype=np.float32),
    }
    arrays = {name: np.ascontiguousarray(a) for name, a in arrays.items()}
    nc = bacc.Bacc("TRN2", target_bir_lowering=False, num_devices=1)
    args = [nc.dram_tensor(name, a.shape, F32, kind="ExternalInput").ap() for name, a in arrays.items()]
    out = nc.dram_tensor("out_t", (2, H, BATCH), F32, kind="ExternalOutput").ap()
    build(nc, *args, out)
    got = run_bass_kernel_spmd(nc, [arrays], core_ids=[0]).results[0]["out_t"]
    return np.ascontiguousarray(got.transpose(2, 0, 1).reshape(BATCH, 2 * H))
```

```python
from contextlib import ExitStack

import numpy as np

import concourse.bass as bass
from concourse import mybir

F32 = mybir.dt.float32
ACT = mybir.ActivationFunctionType
ALU = mybir.AluOpType

BATCH, M, K = 512, 26, 32
H = 128
MC = M + 1
BL = 128 // K
GROUPS = BATCH // BL
GB = 16
BLOCKS = GROUPS // GB
HALF = M // 2

DIAG = 0
RUN = {b: HALF + b * (b - 1) // 2 for b in range(1, HALF + 1)}
INNER = RUN[HALF]
SIZES = [INNER, INNER + HALF + 1]
COLS = [0, SIZES[0]]
PAIRS = sum(SIZES)
CROSS = HALF * HALF
CROSS_ROWS = 128 // HALF
CROSS_TILES = -(-HALF // CROSS_ROWS)

BANK = 512
BANKS = 8
WIDTH = BL * MC
PER_BANK = BANK // WIDTH
FILLS = 2 * GB // PER_BANK
D_PER_BANK = BANK // CROSS
C_PER_BANK = BANK // H
D_FILLS = [list(range(j, min(j + D_PER_BANK, M))) for j in range(0, M, D_PER_BANK)]
C_FILLS = [(n, s, min(s + C_PER_BANK, M)) for n in range(2) for s in range(0, M, C_PER_BANK)]
BLOCK0_FILL = len(D_FILLS)
C_FILL = BLOCK0_FILL + FILLS
REST_FILL = C_FILL + len(C_FILLS) - FILLS
assert GB % PER_BANK == 0 and FILLS % BANKS == 0 and max(SIZES) <= 128


def build(nc, x_cols, w_pairs, w1_t, w2_t, b2, eye, out_t):
    with ExitStack() as ctx:
        def sb(name, shape):
            return ctx.enter_context(nc.sbuf_tensor(name, shape, F32))

        def sem(name):
            return ctx.enter_context(nc.semaphore(name))

        x_dense = sb("x_dense", [128, GROUPS, MC])
        x_diag = sb("x_diag", [128, 2, BL, GB, MC])
        slot0 = sb("slot0", [128, GB * PAIRS])
        slot1 = sb("slot1", [128, GB * PAIRS])
        prods = [s[:, :].rearrange("p (g n) -> p g n", n=PAIRS) for s in (slot0, slot1)]
        moments = sb("moments", [128, 2 * MC, BATCH])
        w_sum = sb("w_sum", [128, PAIRS + CROSS])
        u_t = sb("u_t", [128, 2 + CROSS_TILES, H])
        w2s = sb("w2s", [128, M, H])
        ident = sb("ident", [128, H])
        b2_raw = sb("b2_raw", [128, 1])
        b2_k = sb("b2_k", [128, 1])
        coef = sb("coef", [128, 2 * M, H])
        ps = ctx.enter_context(nc.psum_tensor("ps", [128, BANKS, BANK], F32))

        NW, NU = 2 * (PAIRS + CROSS), 2 * (2 + CROSS_TILES) * H
        w_raw = slot1[:, 0:NW].rearrange("p (a n) -> p a n", a=2)
        u_t_raw = slot1[:, NW:NW + NU].rearrange("p (a n h) -> p a n h", a=2, h=H)
        late = BATCH // 2
        d_sb = moments[:, 0:M, late:late + CROSS].rearrange("p j (a b) -> p j a b", b=HALF)
        moved = [moments[:, M + HALF * n:M + HALF * (n + 1), late:late + SIZES[n]] for n in range(2)]
        cross = w2s[:, :, :].rearrange("p j h -> p (j h)")[:, 0:CROSS_TILES * BATCH].rearrange(
            "p (t b) -> p t b", b=BATCH)
        res = slot0[:, 0:2 * BATCH].rearrange("p (a b) -> p a b", a=2)

        w_loaded = sem("w_loaded")
        w2_loaded = sem("w2_loaded")
        small_loaded = sem("small_loaded")
        x_first = sem("x_first")
        x_rest = sem("x_rest")
        diag_zeroed = sem("diag_zeroed")
        diag_loaded = [sem("diag_loaded0"), sem("diag_loaded1")]
        w_summed = sem("w_summed")
        moved_zeroed = sem("moved_zeroed")
        moved_ready = sem("moved_ready")
        prods_ready = sem("prods_ready")
        weights_filled = sem("weights_filled")
        filled = sem("filled")
        evacuated = sem("evacuated")
        cross_ready = sem("cross_ready")
        first_sum = sem("first_sum")
        second_sum = sem("second_sum")
        b2_ready = sem("b2_ready")
        res_ready = sem("res_ready")
        stored = sem("stored")

        def bank(n):
            return ps[:, n % BANKS, :]

        block = ctx.enter_context(nc.Block())

        @block.sync
        def _(sp):
            def load_diag(t, slot):
                for bl in range(BL):
                    rows = slice(K * bl, K * (bl + 1))
                    sp.dma_start(x_diag[rows, slot, bl].rearrange("p g m -> p (g m)"),
                                 x_cols[rows, bass.ds(t * (GB * MC), GB * MC)]).then_inc(diag_loaded[slot], 16)

            flat = x_dense[:, :, :].rearrange("p g m -> p (g m)")
            sp.dma_start(slot1[:, 0:NW], w_pairs).then_inc(w_loaded, 16)
            sp.dma_start(flat[:, 0:GB * MC], x_cols[:, 0:GB * MC]).then_inc(x_first, 16)
            for slot in range(2):
                sp.wait_ge(diag_zeroed, slot + 1)
                load_diag(slot, slot)
            sp.dma_start(flat[:, GB * MC:], x_cols[:, GB * MC:]).then_inc(x_rest, 16)
            with sp.Fori(1, BLOCKS // 2) as i:
                for slot in range(2):
                    sp.wait_ge(filled, i * (2 * FILLS) + (slot - 1) * FILLS)
                    load_diag(2 * i + slot, slot)
            sp.wait_ge(evacuated, REST_FILL + FILLS * BLOCKS)
            for a in range(HALF):
                r = a % CROSS_ROWS * HALF
                sp.dma_start(cross[r:r + HALF, a // CROSS_ROWS, :],
                             moments[INNER:INNER + HALF, MC + a, :]).then_inc(cross_ready, 16)
            for n in (1, 0):
                sp.wait_ge(res_ready, 2 - n)
                sp.dma_start(out_t[n], res[:, n, :]).then_inc(stored, 16)
            sp.wait_ge(stored, 32)

        @block.gpsimd
        def _(pool):
            for slot in range(2):
                nc.gpsimd.memset(x_diag[:, slot], 0.0).then_inc(diag_zeroed, 1)

            nc.gpsimd.memset(moved[1][:, :, INNER:], 0.0).then_inc(moved_zeroed, 1)

        @block.vector
        def _(dve):
            def pair_products(t, slot):
                x = x_dense[:, bass.ds(t * GB, GB), :]
                for n in range(2):
                    if not isinstance(t, int):
                        dve.wait_ge(filled, t * FILLS + ((n + 1) * (FILLS // 2) - 2 * FILLS))
                    lo = n * HALF
                    out = prods[slot][:, :, COLS[n]:COLS[n] + SIZES[n]]
                    last = nc.vector.tensor_tensor(out[:, :, DIAG:DIAG + HALF], x[:, :, lo:lo + HALF],
                                                   x[:, :, lo:lo + HALF], ALU.mult)
                    for b in range(1, HALF + n):
                        w = b + (b == HALF)
                        last = nc.vector.tensor_tensor(
                            out[:, :, RUN[b]:RUN[b] + w], x[:, :, lo:lo + w],
                            x[:, :, lo + b:lo + b + 1].to_broadcast([128, GB, w]), ALU.mult)
                    last.then_inc(prods_ready, 1)

            dve.wait_ge(w_loaded, 16)
            nc.vector.tensor_tensor(w_sum[:, :], w_raw[:, 0, :], w_raw[:, 1, :], ALU.add).then_inc(w_summed, 1)
            dve.wait_ge(x_first, 16)
            pair_products(0, 0)
            dve.wait_ge(small_loaded, 48)
            nc.vector.tensor_tensor(u_t[:, :, :], u_t_raw[:, 0], u_t_raw[:, 1], ALU.add).then_inc(w_summed, 1)
            nc.vector.tensor_scalar(b2_k[:, :], b2_raw[:, :], float(K), None, ALU.mult).then_inc(b2_ready, 1)

            dve.wait_ge(evacuated, BLOCK0_FILL)
            for n in range(2):
                step, inner = (HALF, 1) if n == 0 else (1, HALF)
                nc.vector.tensor_copy(
                    moved[n][:, :, DIAG:DIAG + HALF].rearrange("p s a -> p a s"),
                    bass.AP(tensor=moments, offset=late + n * HALF * BATCH,
                            ap=[[2 * MC * BATCH, 128], [BATCH + step, HALF], [inner, HALF]]))
                for c in range(1, HALF):
                    out = moved[n][:, :, RUN[c]:RUN[c] + c]
                    if n == 0:
                        one = d_sb[:, c, 0:c, :].rearrange("p a b -> p b a")
                        other = d_sb[:, 0:c, c, :].rearrange("p a b -> p b a")
                    else:
                        one = d_sb[:, HALF + c, :, 0:c]
                        other = d_sb[:, HALF:HALF + c, :, c].rearrange("p b a -> p a b")
                    last = nc.vector.tensor_tensor(out, one, other, ALU.add)
            last.then_inc(moved_ready, 1)
            dve.wait_ge(w_summed, 2)
            dve.wait_ge(x_rest, 16)
            pair_products(1, 1)
            with dve.Fori(1, BLOCKS // 2) as i:
                for slot in range(2):
                    pair_products(2 * i + slot, slot)

        @block.tensor
        def _(pe):
            def block_moments(slot, first_bank, fill, ready, diag_count):
                pe.wait_ge(diag_loaded[slot], diag_count)
                f = 0
                for n in range(2):
                    pe.wait_ge(prods_ready, ready + n)
                    for q in range(GB // PER_BANK):
                        pe.wait_ge(evacuated, fill + (f + 1 - BANKS))
                        for g in range(PER_BANK):
                            gg = q * PER_BANK + g
                            last = nc.tensor.matmul(
                                bank(first_bank + f)[0:SIZES[n], g * WIDTH:(g + 1) * WIDTH],
                                prods[slot][:, gg, COLS[n]:COLS[n] + SIZES[n]],
                                x_diag[:, slot, :, gg, :], start=True, stop=True)
                        last.then_inc(filled, 1)
                        f += 1

            pe.wait_ge(w_summed, 1)
            pe.wait_ge(w2_loaded, 16)
            for n, js in enumerate(D_FILLS):
                if n >= BANKS:
                    pe.wait_ge(evacuated, n - BANKS + 1)
                for s, j in enumerate(js):
                    last = nc.tensor.matmul(bank(n)[:, s * CROSS:(s + 1) * CROSS], w2s[:, j, :],
                                            w_sum[:, PAIRS:PAIRS + CROSS], start=True, stop=True)
                last.then_inc(weights_filled, 1)

            block_moments(0, BLOCK0_FILL, BLOCK0_FILL, 1, 16 * BL)

            pe.wait_ge(small_loaded, 48)
            pe.wait_ge(moved_zeroed, 1)
            pe.wait_ge(moved_ready, 1)
            for m, (n, s0, s1) in enumerate(C_FILLS):
                pe.wait_ge(evacuated, C_FILL + m - BANKS + 1)
                out = bank(C_FILL + m)
                takers = [s for s in range(s0, s1) if (s < HALF) == (n == 1)]
                last = nc.tensor.matmul(out[0:SIZES[n], 0:(s1 - s0) * H], w_sum[:, COLS[n]:COLS[n] + SIZES[n]],
                                        w2s[:, s0:s1, :], start=True, stop=not takers)
                for s in takers:
                    last = nc.tensor.matmul(out[0:SIZES[n], (s - s0) * H:(s - s0 + 1) * H],
                                            moved[n][:, s % HALF, :], ident[:, :],
                                            start=False, stop=s == takers[-1])
                last.then_inc(weights_filled, 1)

            block_moments(1, REST_FILL, REST_FILL + FILLS, 3, 16 * BL)
            with pe.Fori(1, BLOCKS // 2) as i:
                for slot in range(2):
                    block_moments(slot, REST_FILL, i * (2 * FILLS) + (REST_FILL + FILLS * slot),
                                  i * 4 + (2 * slot + 1), (i + 1) * (16 * BL))

            pe.wait_ge(w_summed, 2)
            pe.wait_ge(evacuated, REST_FILL + FILLS * BLOCKS)
            for n in range(2):
                for s in range(M):
                    last = nc.tensor.matmul(ps[:, 1, :], coef[0:SIZES[n], M * n + s, :],
                                            moments[0:SIZES[n], MC * n + s, :],
                                            start=n == 0 and s == 0, stop=n == 1 and s == M - 1)
            last.then_inc(second_sum, 1)
            for n in range(2):
                nc.tensor.matmul(ps[:, 0, :], u_t[0:SIZES[n], n, :], moments[0:SIZES[n], MC * n + M, :],
                                 start=n == 0, stop=False)
            pe.wait_ge(cross_ready, 16 * HALF)
            for t in range(CROSS_TILES):
                rows = HALF * min(CROSS_ROWS, HALF - t * CROSS_ROWS)
                last = nc.tensor.matmul(ps[:, 0, :], u_t[0:rows, 2 + t, :], cross[0:rows, t, :],
                                        start=False, stop=t == CROSS_TILES - 1)
            last.then_inc(first_sum, 1)

        @block.scalar
        def _(act):
            act.dma_start(w2s[:, :, :].rearrange("p j h -> p (j h)"), w2_t).then_inc(w2_loaded, 16)
            act.dma_start(slot1[:, NW:NW + NU], w1_t).then_inc(small_loaded, 16)
            act.dma_start(ident[:, :], eye).then_inc(small_loaded, 16)
            act.dma_start(b2_raw[:, :], b2).then_inc(small_loaded, 16)

            def keep_moments(t, first_bank):
                nb = PER_BANK * BL
                f = 0
                for n in range(2):
                    for q in range(GB // PER_BANK):
                        act.wait_ge(filled, t * FILLS + (f + 1))
                        nc.scalar.activation(
                            moments[0:SIZES[n], MC * n:MC * (n + 1), bass.ds(t * (GB * BL) + q * nb, nb)],
                            bank(first_bank + f)[0:SIZES[n], 0:PER_BANK * WIDTH].rearrange(
                                "p (b m) -> p m b", m=MC), ACT.Copy).then_inc(evacuated, 1)
                        f += 1

            for n, js in enumerate(D_FILLS):
                act.wait_ge(weights_filled, n + 1)
                nc.scalar.activation(
                    moments[:, js[0]:js[-1] + 1, late:late + CROSS],
                    bank(n)[:, 0:CROSS * len(js)].rearrange("p (j w) -> p j w", w=CROSS),
                    ACT.Copy).then_inc(evacuated, 1)
            keep_moments(0, BLOCK0_FILL)
            for m, (n, s0, s1) in enumerate(C_FILLS):
                act.wait_ge(weights_filled, len(D_FILLS) + m + 1)
                nc.scalar.activation(
                    coef[0:SIZES[n], M * n + s0:M * n + s1, :].rearrange("p s h -> p (s h)"),
                    bank(C_FILL + m)[0:SIZES[n], 0:(s1 - s0) * H], ACT.Copy).then_inc(evacuated, 1)
            keep_moments(1, REST_FILL)
            with act.Fori(1, BLOCKS // 2) as i:
                for slot in range(2):
                    keep_moments(2 * i + slot, REST_FILL)
            act.wait_ge(b2_ready, 1)
            act.wait_ge(second_sum, 1)
            nc.scalar.activation(res[:, 1, :], ps[:, 1, :], ACT.Identity,
                                 bias=b2_k[:, 0:1]).then_inc(res_ready, 1)
            act.wait_ge(first_sum, 1)
            nc.scalar.activation(res[:, 0, :], ps[:, 0, :], ACT.Copy).then_inc(res_ready, 1)


def kernel(r_inputs, L0_rec_W1, L0_rec_b1, L0_rec_W2, L0_rec_b2):
    import concourse.bacc as bacc
    from concourse.bass_utils import run_bass_kernel_spmd

    x, w1, b1, w2, b2 = (np.asarray(a) for a in (r_inputs, L0_rec_W1, L0_rec_b1, L0_rec_W2, L0_rec_b2))
    x_cols = np.ones((BL, K, GROUPS, MC), np.float32)
    x_cols[..., :M] = x.reshape(GROUPS, BL, M, K).transpose(1, 3, 0, 2)
    pairs = np.zeros((2, H, PAIRS + CROSS), np.float32)
    for n, lo in enumerate((0, HALF)):
        for b in range(HALF):
            pairs[0, :, COLS[n] + DIAG + b] = w1[:, lo + b, lo + b]
            if b:
                at = COLS[n] + RUN[b]
                pairs[0, :, at:at + b] = w1[:, lo:lo + b, lo + b]
                pairs[1, :, at:at + b] = w1[:, lo + b, lo:lo + b]
    pairs[0, :, PAIRS - 1] = b1
    pairs[0, :, PAIRS:] = w1[:, :HALF, HALF:].reshape(H, CROSS)
    pairs[1, :, PAIRS:] = w1[:, HALF:, :HALF].transpose(0, 2, 1).reshape(H, CROSS)
    w1_t = np.zeros((128, 2, 2 + CROSS_TILES, H), np.float32)
    for n in range(2):
        w1_t[:SIZES[n], :, n, :] = pairs[:, :, COLS[n]:COLS[n] + SIZES[n]].transpose(2, 0, 1)
    for t in range(CROSS_TILES):
        part = pairs[:, :, PAIRS + t * CROSS_ROWS * HALF:PAIRS + min(CROSS, (t + 1) * CROSS_ROWS * HALF)]
        w1_t[:part.shape[2], :, 2 + t, :] = part.transpose(2, 0, 1)
    arrays = {
        "x_cols": x_cols.reshape(128, GROUPS * MC),
        "w_pairs": pairs.transpose(1, 0, 2).reshape(H, -1),
        "w1_t": w1_t.reshape(128, -1),
        "w2_t": w2.transpose(1, 2, 0).reshape(H, M * H),
        "b2": b2.reshape(H, 1),
        "eye": np.eye(H, dtype=np.float32),
    }
    arrays = {name: np.ascontiguousarray(a) for name, a in arrays.items()}
    nc = bacc.Bacc("TRN2", target_bir_lowering=False, num_devices=1)
    args = [nc.dram_tensor(name, a.shape, F32, kind="ExternalInput").ap() for name, a in arrays.items()]
    out = nc.dram_tensor("out_t", (2, H, BATCH), F32, kind="ExternalOutput").ap()
    build(nc, *args, out)
    got = run_bass_kernel_spmd(nc, [arrays], core_ids=[0]).results[0]["out_t"]
    return np.ascontiguousarray(got.transpose(2, 0, 1).reshape(BATCH, 2 * H))
```

```python
from contextlib import ExitStack

import numpy as np

import concourse.bass as bass
from concourse import mybir

F32 = mybir.dt.float32
F32R = mybir.dt.float32r
ACT = mybir.ActivationFunctionType
ALU = mybir.AluOpType

BATCH, M, K = 512, 26, 32
H = 128
MC = M + 1
BL = 128 // K
GROUPS = BATCH // BL
GB = 16
BLOCKS = GROUPS // GB
HALF = M // 2


def tri(n):
    return n * (n + 1) // 2


FIELD_PAIRS = tri(HALF)
SIZES = [FIELD_PAIRS, FIELD_PAIRS + 1 + HALF]
CC = FIELD_PAIRS
COLS = [0, SIZES[0]]
PAIRS = sum(SIZES)
CROSS = HALF * HALF
W_SIZES = [FIELD_PAIRS, FIELD_PAIRS + 1]
W_COLS = [0, FIELD_PAIRS + CROSS]
WEIGHTS = sum(W_SIZES) + CROSS
W_ROWS = -(-WEIGHTS // 128)
PART = 4
W2_LOADS = [(0, M // PART // 2 * PART), (M // PART // 2 * PART, M)]
W2_PARTS = [(j, min(j + PART, M)) for j in range(0, M, PART)]

PLACE = [128 - FIELD_PAIRS, 128]
INNER_ORDER = [[[12, 9], [11, 10], [8, 6], [7, 0], [5, 4], [3, 2, 1]],
               [[12, 7, 0], [11, 8, 1], [10, 9, 2], [6, 5, 4, 3]]]


def inner_starts(n):
    starts, ends, at = {}, [], 0
    for ks in INNER_ORDER[n]:
        for k in ks:
            starts[k] = at
            at += tri(k + 1)
        while len(ends) * PLACE[n] < at:
            ends.append(min((len(ends) + 1) * PLACE[n], at))
        at = len(ends) * PLACE[n]
    return starts, ends


def common_pieces(starts, cuts):
    return [(max(a0, b0), min(a1, b1), i, t)
            for i, (a0, a1) in enumerate(zip(starts, starts[1:]))
            for t, (b0, b1) in enumerate(zip(cuts, cuts[1:])) if max(a0, b0) < min(a1, b1)]


def inner_moves(n):
    moves, size = [], PLACE[n]
    for k, at in INNER_AT[n].items():
        for t in range(at // size, (at + tri(k + 1) - 1) // size + 1):
            first, end = max(at, t * size), min(at + tri(k + 1), (t + 1) * size)
            moves.append((first - at, end - at, k, t, first - t * size))
    return sorted(moves, key=lambda move: move[3:])


INNER_AT = [inner_starts(n)[0] for n in range(2)]
INNER_ROWS = [[end - t * PLACE[n] for t, end in enumerate(inner_starts(n)[1])] for n in range(2)]
INNER_MOVES = [inner_moves(n) for n in range(2)]
assert all(sorted(at) == list(range(HALF)) for at in INNER_AT)
HIGH_TILES = len(INNER_ROWS[1])
LOW_ROWS = [FIELD_PAIRS + rows for rows in INNER_ROWS[0]]
INNER_SUMS = [len(rows) * place for rows, place in zip(INNER_ROWS, PLACE)]
SECOND_ROW = [SIZES[0], SIZES[1], 0]
SECOND_CUTS = [0, 128 - SIZES[0], (256 - PAIRS) // HALF * HALF, CROSS]
SECOND_MOVES = common_pieces([HALF * a for a in range(HALF + 1)], SECOND_CUTS)
SECOND_ROWS = [row + c1 - c0 for row, c0, c1 in zip(SECOND_ROW, SECOND_CUTS, SECOND_CUTS[1:])]
assert len(LOW_ROWS) == HALF and max(SECOND_ROWS) <= 128

BANK = 512
BANKS = 8
WIDTH = BL * MC
PER_BANK = BANK // WIDTH
FILLS = 2 * GB // PER_BANK
C_PER_BANK = BANK // H
SLOTS = [HALF, HALF + 1]
LOW_FILLS = [(s, min(s + C_PER_BANK, HALF)) for s in range(0, HALF, C_PER_BANK)]
C_FILLS = LOW_FILLS + [(HALF, HALF + 1)]
D_FILL = FILLS
BLOCK1_FILL = D_FILL + M
C_FILL = BLOCK1_FILL + FILLS
REST_FILL = C_FILL + len(C_FILLS) - 2 * FILLS
SUM_BANKS = [REST_FILL % BANKS, (REST_FILL + 1) % BANKS]
C_EVACUATED = C_FILL + M
REST_EVACUATED = REST_FILL + M
INNER_EVACUATED = REST_EVACUATED + FILLS * BLOCKS
HIGH_EVACUATED = INNER_EVACUATED - FILLS // 2
INNER_FILL = REST_FILL + FILLS * BLOCKS + 2
WHOLE = 8
LOW_SPLIT = SLOTS[1] - WHOLE
INNER_SPLIT = LOW_SPLIT + HALF
SPLIT = INNER_SPLIT + HIGH_TILES
SPLIT_ROWS = [W_SIZES[1]] * (HALF - WHOLE) + [SIZES[1]] + LOW_ROWS + INNER_ROWS[1]
SPLIT_GROUPS = ([(0, LOW_SPLIT - 1, W_SIZES[1]), (LOW_SPLIT - 1, LOW_SPLIT, SIZES[1])]
                + [(LOW_SPLIT + s0, LOW_SPLIT + s1, 128) for s0, s1 in LOW_FILLS] + [(INNER_SPLIT, SPLIT, 128)])
RING = 4
FOR_LOW = RING
FOR_INNER = 8
X1_PLACE = 7
X1_KEPT = 16
LOW_TURN = 2
INNER_TURN = 6
assert len(W2_PARTS) < FILLS
assert GB % PER_BANK == 0 and FILLS % BANKS == 0 and max(SIZES) <= 128 and HIGH_TILES <= C_PER_BANK


def build(nc, x_cols, w_pairs, w1_t, w2_t, b2, eye, factors, out_t):
    with ExitStack() as ctx:
        def sb(name, shape, dtype=F32):
            return ctx.enter_context(nc.sbuf_tensor(name, shape, dtype))

        def sem(name):
            return ctx.enter_context(nc.semaphore(name))

        x_dense = sb("x_dense", [128, GROUPS, MC])
        x_diag = sb("x_diag", [128, 2, BL, GB, MC])
        moments = sb("moments", [128, 2 * MC, BATCH])
        w_hi = sb("w_hi", [128, W_ROWS, 128], F32R)
        w_lo = sb("w_lo", [128, W_ROWS, 128], F32R)
        u_t = sb("u_t", [128, 3, H])
        ident = sb("ident", [128, H])
        b2_raw = sb("b2_raw", [128, 1])
        b2_k = sb("b2_k", [128, 1])
        warm = sb("warm", [128, 1])
        factor = sb("factor", [128, HALF + 1 + HIGH_TILES])
        d_own = [sb(f"d_own{n}", [128, HALF, W_SIZES[n]]) for n in range(2)]
        with (nc.sbuf_tensor("w2_hi", [128, M, H], F32R) as w2_hi,
              nc.sbuf_tensor("w2_lo", [128, M, H], F32R) as w2_lo):
            pass
        low_sum = sb("low_sum", [128, HALF, 128])
        coef = sb("coef", [128, SLOTS[1], H])
        res = sb("res", [128, 2, BATCH])
        coef_hi = sb("coef_hi", [128, SPLIT, H], F32R)
        with (nc.sbuf_tensor("coef_lo", [128, SPLIT, H], F32R) as coef_lo,
              nc.sbuf_tensor("value_hi", [128, RING, BATCH], F32R) as value_hi,
              nc.sbuf_tensor("value_lo", [128, RING, BATCH], F32R) as value_lo):
            pass
        prods = [sb(f"prods{slot}", [128, GB, PAIRS]) for slot in range(2)]
        ps = ctx.enter_context(nc.psum_tensor("ps", [128, BANKS, BANK], F32))

        early = 2 * GB * BL
        raw = moments[:, :, early:early + H]
        w2_raw = raw[:, 0:M, :]
        w_raw = raw[:, M:M + 2 * W_ROWS, :]
        w_sum = w_raw[:, 0:W_ROWS, :]
        u_t_raw = raw[:, M + 2 * W_ROWS:M + 2 * W_ROWS + 6, :]
        late = BATCH // 2
        d_cross = moments[:, 0:M, late:late + CROSS].rearrange("p j (a b) -> p j a b", b=HALF)
        d_other = [moments[:, M + HALF * (1 - n):M + HALF * (2 - n),
                           late + SIZES[1]:late + SIZES[1] + W_SIZES[n]]
                   for n in range(2)]
        high_sum = moments[:, M + HALF:M + HALF + SLOTS[1], late:late + SIZES[1]]
        second = x_diag[:, 0].rearrange("p a g m -> p (a g m)")[:, 0:BATCH]
        inner_sums = res[:, :, :].rearrange("p a b -> p (a b)")[:, 0:sum(INNER_SUMS)]
        inner_sum = [inner_sums[:, 0:INNER_SUMS[0]], inner_sums[:, INNER_SUMS[0]:]]
        NG = HIGH_TILES * BATCH
        x_flat = x_dense[:, :, :].rearrange("p g m -> p (g m)")
        gathered = x_flat[:, 0:NG].rearrange("p (t b) -> p t b", b=BATCH)

        def split_values(u, rows):
            if u < LOW_SPLIT:
                return moments[0:rows, MC + high_third(WHOLE + u), :]
            return moments[0:rows, HALF + u - LOW_SPLIT, :] if u < INNER_SPLIT else gathered[0:rows, u - INNER_SPLIT, :]

        def high_third(s):
            return s if s < HALF else M

        low_coef = x_diag[:, 1].rearrange("p a g m -> p (a g m)")[:, 0:HALF * H].rearrange("p (s h) -> p s h", h=H)
        inner_coef = x_flat[:, NG:NG + HIGH_TILES * H].rearrange("p (s h) -> p s h", h=H)

        def split_coefs(u0, u1):
            if u0 < LOW_SPLIT:
                return coef[:, WHOLE + u0:WHOLE + u1, :]
            if u0 < INNER_SPLIT:
                return low_coef[:, u0 - LOW_SPLIT:u1 - LOW_SPLIT, :]
            return inner_coef[:, u0 - INNER_SPLIT:u1 - INNER_SPLIT, :]

        w_loaded = sem("w_loaded")
        w2_loaded = [sem("w2_loaded0"), sem("w2_loaded1")]
        w2_hi_ready = sem("w2_hi_ready")
        w2_lo_ready = sem("w2_lo_ready")
        small_loaded = sem("small_loaded")
        x_first = [sem("x_first0"), sem("x_first1")]
        x_second = sem("x_second")
        x_rest = sem("x_rest")
        diag_zeroed = sem("diag_zeroed")
        diag_copied = sem("diag_copied")
        diag_loaded = [sem("diag_loaded0"), sem("diag_loaded1")]
        w_split = sem("w_split")
        u_ready = sem("u_ready")
        constant_zeroed = sem("constant_zeroed")
        cross_part = sem("cross_part")
        own_kept = sem("own_kept")
        inner_zeroed = sem("inner_zeroed")
        inner_part = [sem("inner_part0"), sem("inner_part1")]
        inner_ready = [sem("inner_ready0"), sem("inner_ready1")]
        low_ready = sem("low_ready")
        gathered_low = [sem(f"gathered_low{m}") for m in range(len(LOW_FILLS))]
        gathered_high = sem("gathered_high")
        ones_set = sem("ones_set")
        high_summed = sem("high_summed")
        low_summed = sem("low_summed")
        high_prods0 = sem("high_prods0")
        low_prods0 = sem("low_prods0")
        prods_ready = sem("prods_ready")
        weights_filled = sem("weights_filled")
        filled = sem("filled")
        evacuated = sem("evacuated")
        cross_ready = sem("cross_ready")
        coef_hi_ready = sem("coef_hi_ready")
        coef_lo_ready = sem("coef_lo_ready")
        value_hi_ready = sem("value_hi_ready")
        value_lo_ready = sem("value_lo_ready")
        value_used = sem("value_used")
        first_sum = sem("first_sum")
        b2_ready = sem("b2_ready")
        res_ready = sem("res_ready")
        stored = sem("stored")

        def bank(n):
            return ps[:, n % BANKS, :]

        def half_products(eng, t, slot, n, g0=0, g1=GB):
            x = x_dense[:, bass.ds(t * GB + g0, g1 - g0), :]
            lo = n * HALF
            out = prods[slot][:, g0:g1, COLS[n]:COLS[n] + SIZES[n]]
            for b in range(HALF):
                last = eng.tensor_tensor(
                    out[:, :, tri(b):tri(b + 1)], x[:, :, lo:lo + b + 1],
                    x[:, :, lo + b:lo + b + 1].to_broadcast([128, g1 - g0, b + 1]), ALU.mult)
            if n:
                last = eng.tensor_tensor(
                    out[:, :, CC + 1:], x[:, :, HALF:M],
                    x[:, :, M:MC].to_broadcast([128, g1 - g0, HALF]), ALU.mult)
            return last

        def inner_coefs(eng, queue, n):
            d = d_own[n]
            for k in range(HALF):
                for j in range(k + 1):
                    at = INNER_AT[n][k] + tri(j)
                    last = eng.tensor_tensor(inner_sum[n][:, at:at + j + 1], d[:, j, tri(k):tri(k) + j + 1],
                                             d[:, 0:j + 1, tri(k) + j], ALU.add)
            last.then_inc(inner_part[n], 1)
            queue.wait_ge(inner_part[n], 1)
            for k in range(HALF):
                part = inner_sum[n][:, INNER_AT[n][k]:INNER_AT[n][k] + tri(k + 1)]
                last = eng.tensor_tensor(part, part, d[:, k, 0:tri(k + 1)], ALU.add)
            last.then_inc(inner_ready[n], 1)

        block = ctx.enter_context(nc.Block())

        @block.sync
        def _(sp):
            def load_diag(t, slot):
                for bl in range(BL):
                    rows = slice(K * bl, K * (bl + 1))
                    sp.dma_start(x_diag[rows, slot, bl].rearrange("p g m -> p (g m)"),
                                 x_cols[rows, bass.ds(t * (GB * MC), GB * MC)]).then_inc(diag_loaded[slot], 16)

            for part in range(2):
                columns = slice(part * (GB // 2 * MC), (part + 1) * (GB // 2 * MC))
                sp.dma_start(x_flat[:, columns], x_cols[:, columns]).then_inc(x_first[part], 16)
            sp.dma_start(w_raw, w_pairs.rearrange("p (r c) -> p r c", c=128)).then_inc(w_loaded, 16)
            sp.dma_start(x_flat[:, GB * MC:2 * GB * MC], x_cols[:, GB * MC:2 * GB * MC]).then_inc(x_second, 16)
            for part, (j0, j1) in enumerate(W2_LOADS):
                sp.dma_start(w2_raw[:, j0:j1, :], w2_t[:, j0 * H:j1 * H].rearrange("p (r c) -> p r c", c=H)
                             ).then_inc(w2_loaded[part], 16)
            sp.dma_start(u_t_raw, w1_t.rearrange("p (r c) -> p r c", c=H)).then_inc(small_loaded, 16)
            sp.dma_start(ident[:, :], eye).then_inc(small_loaded, 16)
            sp.dma_start(b2_raw[:, :], b2).then_inc(small_loaded, 16)
            sp.dma_start(factor[:, :], factors).then_inc(small_loaded, 16)
            sp.wait_ge(diag_zeroed, 2)
            load_diag(1, 1)
            sp.dma_start(x_flat[:, 2 * GB * MC:], x_cols[:, 2 * GB * MC:]).then_inc(x_rest, 16)
            with sp.Fori(1, BLOCKS // 2) as i:
                for slot in range(2):
                    sp.wait_ge(filled, i * (2 * FILLS) + (slot - 1) * FILLS)
                    load_diag(2 * i + slot, slot)

            def gather_high(moves):
                for r0, r1, k, t, row in moves:
                    sp.dma_start(gathered[row:row + r1 - r0, t, :], moments[r0:r1, MC + HALF + k, :]
                                 ).then_inc(gathered_high, 16)

            sp.wait_ge(prods_ready, 2 * (BLOCKS - 1))
            sp.wait_ge(evacuated, HIGH_EVACUATED)
            gather_high([move for move in INNER_MOVES[1] if move[3] == 0])
            sp.wait_ge(evacuated, INNER_EVACUATED)
            for r0, r1, k, t, row in INNER_MOVES[0]:
                row += FIELD_PAIRS
                sp.dma_start(moments[row:row + r1 - r0, HALF + t, :], moments[r0:r1, k, :]
                             ).then_inc(gathered_low[t // C_PER_BANK], 16)
            gather_high([move for move in INNER_MOVES[1] if move[3] > 0])
            for n in range(2):
                sp.wait_ge(res_ready, n + 1)
                sp.dma_start(out_t[n], res[:, n, :]).then_inc(stored, 16)
            sp.wait_ge(stored, 32)

        @block.gpsimd
        def _(pool):
            nc.gpsimd.memset(x_diag[:, 0], 0.0).then_inc(diag_zeroed, 1)
            for loaded in x_first:
                pool.wait_ge(loaded, 16)
            half_products(nc.gpsimd, 0, 0, 0).then_inc(low_prods0, 1)
            for m, (j0, j1) in enumerate(W2_PARTS):
                pool.wait_ge(w2_hi_ready, m + 1)
                nc.gpsimd.tensor_tensor(w2_lo[:, j0:j1, :], w2_raw[:, j0:j1, :], w2_hi[:, j0:j1, :].bitcast(F32),
                                        ALU.subtract).then_inc(w2_lo_ready, 1)
            nc.gpsimd.memset(x_diag[:, 1], 0.0).then_inc(diag_zeroed, 1)

            nc.gpsimd.memset(high_sum[:, 0:HALF, CC:CC + 1], 0.0).then_inc(constant_zeroed, 1)
            nc.gpsimd.memset(high_sum[:, HALF, 0:CC + 1], 0.0).then_inc(constant_zeroed, 1)
            pool.wait_ge(own_kept, M)
            nc.gpsimd.memset(inner_sums, 0.0).then_inc(inner_zeroed, 1)
            pool.wait_ge(inner_zeroed, 1)
            inner_coefs(nc.gpsimd, pool, 0)
            pool.wait_ge(inner_ready[0], 1)
            pool.wait_ge(low_summed, 1)
            nc.gpsimd.tensor_copy(low_sum[:, :, FIELD_PAIRS:],
                                  inner_sum[0].rearrange("p (s r) -> p s r", r=PLACE[0])).then_inc(low_ready, 1)

            pool.wait_ge(evacuated, HIGH_EVACUATED)
            places = (moments[:, M, :], moments[:, MC + M, :], second)
            for r0, r1, a, t in SECOND_MOVES:
                row = SECOND_ROW[t] + r0 - SECOND_CUTS[t]
                b = CC + 1 + r0 - HALF * a
                pool.dma_start(places[t][row:row + r1 - r0, :],
                               moments[b:b + r1 - r0, MC + a, :]).then_inc(cross_ready, 16)

        @block.vector
        def _(dve):
            for p in prods:
                nc.vector.memset(p[:, :, COLS[1] + CC:COLS[1] + CC + 1], 1.0).then_inc(ones_set, 1)
            for part in range(2):
                dve.wait_ge(x_first[part], 16)
                half_products(nc.vector, 0, 0, 1, part * (GB // 2), (part + 1) * (GB // 2)).then_inc(high_prods0, 1)
            dve.wait_ge(w_loaded, 16)
            nc.vector.tensor_tensor(w_sum, w_sum, w_raw[:, W_ROWS:, :], ALU.add).then_inc(w_split, 1)
            dve.wait_ge(w_split, 1)
            nc.vector.tensor_copy(w_hi[:, :, :], w_sum).then_inc(w_split, 1)
            dve.wait_ge(w_split, 2)
            nc.vector.tensor_tensor(w_lo[:, :, :], w_sum, w_hi[:, :, :].bitcast(F32), ALU.subtract
                                    ).then_inc(w_split, 1)
            dve.wait_ge(x_second, 16)
            for n in (1, 0):
                half_products(nc.vector, 1, 1, n).then_inc(prods_ready, 1)
            dve.wait_ge(small_loaded, 64)
            nc.vector.tensor_tensor(u_t[:, :, :], u_t_raw[:, 0:3, :], u_t_raw[:, 3:6, :], ALU.add).then_inc(u_ready, 1)
            nc.vector.tensor_scalar(b2_k[:, :], b2_raw[:, :], float(K), None, ALU.mult).then_inc(b2_ready, 1)

            for j in range(M):
                n = j // HALF
                dve.wait_ge(evacuated, D_FILL + 2 * (j + 1))
                nc.vector.tensor_copy(
                    d_own[n][:, j % HALF, :],
                    bank(D_FILL + j)[:, W_COLS[n]:W_COLS[n] + W_SIZES[n]]).then_inc(own_kept, 1)
                if n:
                    c = j - HALF
                    nc.vector.tensor_tensor(low_sum[:, :, tri(c):tri(c + 1)],
                                            d_cross[:, c, 0:c + 1, :].rearrange("p a b -> p b a"),
                                            d_cross[:, 0:c + 1, c, :].rearrange("p a b -> p b a"), ALU.add)
                    last = nc.vector.tensor_tensor(high_sum[:, 0:HALF, tri(c):tri(c + 1)],
                                                   d_cross[:, HALF + c, :, 0:c + 1],
                                                   d_cross[:, HALF:HALF + c + 1, :, c].rearrange("p b a -> p a b"),
                                                   ALU.add)
            last.then_inc(cross_part, 1)
            dve.wait_ge(cross_part, 1)
            dve.wait_ge(constant_zeroed, 2)
            dve.wait_ge(own_kept, M)
            nc.vector.tensor_copy(high_sum[:, HALF, CC + 1:], d_own[1][:, :, CC]).then_inc(high_summed, 1)
            for n, sums, summed in ((1, high_sum, high_summed), (0, low_sum, low_summed)):
                part = sums[:, 0:HALF, 0:W_SIZES[n]]
                nc.vector.tensor_tensor(part, part, d_other[n], ALU.add).then_inc(summed, 1)
            dve.wait_ge(x_rest, 16)
            with dve.Fori(1, BLOCKS // 2) as i:
                for slot in range(2):
                    t = 2 * i + slot
                    for f, n in enumerate((1, 0)):
                        dve.wait_ge(filled, t * FILLS + ((f + 1) * (FILLS // 2) - 2 * FILLS))
                        half_products(nc.vector, t, slot, n).then_inc(prods_ready, 1)

            dve.wait_ge(inner_zeroed, 1)
            inner_coefs(nc.vector, dve, 1)

            def coefs_low(groups):
                for g in groups:
                    u0, u1, rows = SPLIT_GROUPS[g]
                    dve.wait_ge(coef_hi_ready, g + 1)
                    nc.vector.tensor_tensor(coef_lo[0:rows, u0:u1, :], split_coefs(u0, u1)[0:rows],
                                            coef_hi[0:rows, u0:u1, :].bitcast(F32), ALU.subtract
                                            ).then_inc(coef_lo_ready, 1)

            dve.wait_ge(evacuated, INNER_EVACUATED)
            coefs_low(range(2))
            for u in range(SPLIT):
                if u == FOR_LOW:
                    coefs_low(range(2, 2 + len(LOW_FILLS)))
                if u == FOR_INNER:
                    coefs_low([2 + len(LOW_FILLS)])
                rows = SPLIT_ROWS[u]
                dve.wait_ge(value_hi_ready, u + 1)
                nc.vector.tensor_tensor(value_lo[0:rows, u % RING, :], split_values(u, rows),
                                        value_hi[0:rows, u % RING, :].bitcast(F32), ALU.subtract
                                        ).then_inc(value_lo_ready, 1)

        @block.tensor
        def _(pe):
            def fill_banks(slot, fills, first_bank, left=None, before=None):
                for f in fills:
                    n = 1 - f // (FILLS // 2)
                    if left is not None:
                        pe.wait_ge(left, before + (f + 1 - BANKS))
                    for g in range(PER_BANK):
                        gg = f % (FILLS // 2) * PER_BANK + g
                        last = nc.tensor.matmul(
                            bank(first_bank + f)[0:SIZES[n], g * WIDTH:(g + 1) * WIDTH],
                            prods[slot][:, gg, COLS[n]:COLS[n] + SIZES[n]],
                            x_diag[:, slot, :, gg, :], start=True, stop=True)
                    last.then_inc(filled, 1)

            def block_moments(slot, first_bank, left, before, ready, diag_count):
                pe.wait_ge(diag_loaded[slot], diag_count)
                for n in range(2):
                    pe.wait_ge(prods_ready, ready + n)
                    fill_banks(slot, range(n * (FILLS // 2), (n + 1) * (FILLS // 2)), first_bank, left, before)

            pe.wait_ge(ones_set, 2)
            for part in range(2):
                pe.wait_ge(diag_copied, (part + 1) * BL)
                pe.wait_ge(high_prods0, part + 1)
                fill_banks(0, range(part * (FILLS // 4), (part + 1) * (FILLS // 4)), 0)
            pe.wait_ge(low_prods0, 1)
            fill_banks(0, range(FILLS // 2, FILLS), 0)

            pe.wait_ge(w_split, 3)
            for j in range(M):
                n = D_FILL + j
                if j % PART == 0:
                    pe.wait_ge(w2_lo_ready, j // PART + 1)
                if j >= BANKS:
                    pe.wait_ge(own_kept, j - BANKS + 1)
                else:
                    pe.wait_ge(evacuated, n - BANKS + 1)
                out = bank(n)[:, 0:WEIGHTS]
                hi, lo = (w[:, :, :].rearrange("p r c -> p (r c)")[:, 0:WEIGHTS] for w in (w_hi, w_lo))
                nc.tensor.matmul(out, w2_hi[:, j, :], hi, start=True, stop=False)
                nc.tensor.matmul(out, w2_hi[:, j, :], lo, start=False, stop=False)
                nc.tensor.matmul(out, w2_lo[:, j, :], hi, start=False, stop=True).then_inc(weights_filled, 1)

            block_moments(1, BLOCK1_FILL, own_kept, M, 1, 16 * BL)

            def turn(fill, pieces):
                for i, piece in enumerate(pieces):
                    last = nc.tensor.transpose(bank(fill)[0:piece.shape[1], i * H:(i + 1) * H], piece,
                                               ident[:, :])
                last.then_inc(weights_filled, 1)

            pe.wait_ge(small_loaded, 64)
            pe.wait_ge(high_summed, 2)
            for m, (s0, s1) in enumerate(C_FILLS):
                pe.wait_ge(evacuated, C_EVACUATED + m - BANKS + 1)
                turn(C_FILL + m, [high_sum[:, s, 0:W_SIZES[1] if s < HALF else SIZES[1]] for s in range(s0, s1)])

            with pe.Fori(1, BLOCKS // 2) as i:
                for slot in range(2):
                    block_moments(slot, REST_FILL, evacuated, i * (2 * FILLS) + (REST_EVACUATED + FILLS * slot),
                                  i * 4 + (2 * slot - 1), (i + slot) * (16 * BL))

            pe.wait_ge(evacuated, HIGH_EVACUATED)
            for s in range(WHOLE):
                if s == LOW_TURN:
                    pe.wait_ge(evacuated, INNER_EVACUATED)
                    pe.wait_ge(low_ready, 1)
                    for m, (s0, s1) in enumerate(LOW_FILLS):
                        turn(INNER_FILL + m, [low_sum[:, l, :] for l in range(s0, s1)])
                if s == INNER_TURN:
                    pe.wait_ge(inner_ready[1], 1)
                    turn(INNER_FILL + len(LOW_FILLS),
                         [inner_sum[1][:, t * 128:(t + 1) * 128] for t in range(HIGH_TILES)])
                nc.tensor.matmul(ps[:, SUM_BANKS[1], :], coef[0:W_SIZES[1], s, :],
                                 moments[0:W_SIZES[1], MC + high_third(s), :], start=s == 0, stop=False)

            for u in range(SPLIT):
                for g, (u0, _, _) in enumerate(SPLIT_GROUPS):
                    if u == u0:
                        pe.wait_ge(coef_lo_ready, g + 1)
                pe.wait_ge(value_lo_ready, u + 1)
                rows, place = SPLIT_ROWS[u], u % RING
                for c, v in ((coef_hi, value_hi), (coef_hi, value_lo), (coef_lo, value_hi)):
                    last = nc.tensor.matmul(ps[:, SUM_BANKS[1], :], c[0:rows, u, :], v[0:rows, place, :],
                                            start=False, stop=u == SPLIT - 1 and c is coef_lo)
                last.then_inc(value_used, 1)
                if u == X1_PLACE:
                    pe.wait_ge(u_ready, 1)
                    pe.wait_ge(cross_ready, 16 * len(SECOND_MOVES))
                    for t, values in enumerate((moments[:, M, :], moments[:, MC + M, :], second)):
                        last = nc.tensor.matmul(ps[:, SUM_BANKS[0], :], u_t[0:SECOND_ROWS[t], t, :],
                                                values[0:SECOND_ROWS[t], :], start=t == 0, stop=t == 2)
                    last.then_inc(first_sum, 1)

        @block.scalar
        def _(act):
            act.wait_ge(ones_set, 2)
            nc.scalar.activation(warm[:, :], prods[1][:, 0, COLS[1] + CC:COLS[1] + CC + 1], ACT.Copy)
            act.wait_ge(diag_zeroed, 1)
            for part in range(2):
                act.wait_ge(x_first[part], 16)
                groups = slice(part * (GB // 2), (part + 1) * (GB // 2))
                for bl in range(BL):
                    rows = slice(K * bl, K * (bl + 1))
                    nc.scalar.activation(x_diag[rows, 0, bl, groups, :], x_dense[rows, groups, :], ACT.Copy
                                         ).then_inc(diag_copied, 1)

            def keep_bank(t, f, first_bank):
                nb = PER_BANK * BL
                n, q = 1 - f // (FILLS // 2), f % (FILLS // 2)
                act.wait_ge(filled, t * FILLS + (f + 1))
                nc.scalar.activation(
                    moments[0:SIZES[n], MC * n:MC * (n + 1), bass.ds(t * (GB * BL) + q * nb, nb)],
                    bank(first_bank + f)[0:SIZES[n], 0:PER_BANK * WIDTH].rearrange("p (b m) -> p m b", m=MC),
                    ACT.Copy).then_inc(evacuated, 1)

            for f in range(FILLS):
                keep_bank(0, f, 0)
                if f and f <= len(W2_PARTS):
                    j0, j1 = W2_PARTS[f - 1]
                    act.wait_ge(w2_loaded[j1 > W2_LOADS[0][1]], 16)
                    nc.scalar.activation(w2_hi[:, j0:j1, :], w2_raw[:, j0:j1, :], ACT.Copy
                                         ).then_inc(w2_hi_ready, 1)
            for j in range(M):
                act.wait_ge(weights_filled, j + 1)
                n = 1 - j // HALF
                nc.scalar.activation(moments[:, j, late:late + CROSS],
                                     bank(D_FILL + j)[:, FIELD_PAIRS:FIELD_PAIRS + CROSS],
                                     ACT.Copy).then_inc(evacuated, 1)
                nc.scalar.activation(d_other[n][:, j % HALF, :],
                                     bank(D_FILL + j)[:, W_COLS[n]:W_COLS[n] + W_SIZES[n]],
                                     ACT.Copy).then_inc(evacuated, 1)
            for f in range(FILLS):
                keep_bank(1, f, BLOCK1_FILL)
            act.wait_ge(small_loaded, 64)
            for m, (s0, s1) in enumerate(C_FILLS):
                act.wait_ge(weights_filled, M + m + 1)
                rows = W_SIZES[1] if s0 < HALF else SIZES[1]
                nc.scalar.activation(
                    coef[0:rows, s0:s1, :].rearrange("p s h -> p (s h)"),
                    bank(C_FILL + m)[0:rows, 0:(s1 - s0) * H], ACT.Copy,
                    scale=factor[0:rows, HALF:HALF + 1]).then_inc(evacuated, 1)

            def coefs_high(g, before):
                u0, u1, rows = SPLIT_GROUPS[g]
                act.wait_ge(evacuated, before)
                nc.scalar.activation(coef_hi[0:rows, u0:u1, :], split_coefs(u0, u1)[0:rows], ACT.Copy
                                     ).then_inc(coef_hi_ready, 1)

            for g in range(2):
                coefs_high(g, REST_EVACUATED + 2 * FILLS)

            with act.Fori(1, BLOCKS // 2) as i:
                for slot in range(2):
                    for f in range(FILLS):
                        keep_bank(2 * i + slot, f, REST_FILL)

            def keep_turned(fill, place, u, column):
                nc.scalar.activation(split_coefs(u, u + 1)[:, 0, :], bank(fill)[:, place * H:(place + 1) * H], ACT.Copy,
                                     scale=factor[:, column:column + 1]).then_inc(evacuated, 1)

            act.wait_ge(evacuated, INNER_EVACUATED)
            for u in range(SPLIT):
                if u == FOR_LOW:
                    for m, (s0, s1) in enumerate(LOW_FILLS):
                        act.wait_ge(weights_filled, M + len(C_FILLS) + m + 1)
                        for s in range(s0, s1):
                            keep_turned(INNER_FILL + m, s - s0, LOW_SPLIT + s, s)
                        coefs_high(2 + m, INNER_EVACUATED + s1)
                if u == FOR_INNER:
                    act.wait_ge(weights_filled, M + len(C_FILLS) + len(LOW_FILLS) + 1)
                    for t in range(HIGH_TILES):
                        keep_turned(INNER_FILL + len(LOW_FILLS), t, INNER_SPLIT + t, HALF + 1 + t)
                    coefs_high(2 + len(LOW_FILLS), INNER_EVACUATED + HALF + HIGH_TILES)
                if u == X1_KEPT:
                    act.wait_ge(first_sum, 1)
                    nc.scalar.activation(res[:, 0, :], ps[:, SUM_BANKS[0], :], ACT.Copy).then_inc(res_ready, 1)
                if LOW_SPLIT <= u < INNER_SPLIT and (u - LOW_SPLIT) % C_PER_BANK == 0:
                    m = (u - LOW_SPLIT) // C_PER_BANK
                    act.wait_ge(gathered_low[m], 16 * sum(t // C_PER_BANK == m for _, _, _, t, _ in INNER_MOVES[0]))
                if u == INNER_SPLIT:
                    act.wait_ge(gathered_high, 16 * len(INNER_MOVES[1]))
                if u >= RING:
                    act.wait_ge(value_used, u - RING + 1)
                rows = SPLIT_ROWS[u]
                nc.scalar.activation(value_hi[0:rows, u % RING, :], split_values(u, rows), ACT.Copy
                                     ).then_inc(value_hi_ready, 1)
            act.wait_ge(b2_ready, 1)
            act.wait_ge(value_used, SPLIT)
            nc.scalar.activation(res[:, 1, :], ps[:, SUM_BANKS[1], :], ACT.Identity,
                                 bias=b2_k[:, 0:1]).then_inc(res_ready, 1)


def kernel(r_inputs, L0_rec_W1, L0_rec_b1, L0_rec_W2, L0_rec_b2):
    import concourse.bacc as bacc
    from concourse.bass_utils import run_bass_kernel_spmd

    x, w1, b1, w2, b2 = (np.asarray(a) for a in (r_inputs, L0_rec_W1, L0_rec_b1, L0_rec_W2, L0_rec_b2))
    x_cols = np.ones((BL, K, GROUPS, MC), np.float32)
    x_cols[..., :M] = x.reshape(GROUPS, BL, M, K).transpose(1, 3, 0, 2)
    pairs = np.zeros((2, H, W_ROWS * 128), np.float32)
    for n, lo in enumerate((0, HALF)):
        for b in range(HALF):
            at = W_COLS[n] + tri(b)
            pairs[0, :, at:at + b + 1] = w1[:, lo:lo + b + 1, lo + b]
            pairs[1, :, at:at + b + 1] = w1[:, lo + b, lo:lo + b + 1]
    pairs[0, :, W_COLS[1] + CC] = b1
    cross = pairs[:, :, FIELD_PAIRS:FIELD_PAIRS + CROSS]
    cross[0] = w1[:, :HALF, HALF:].reshape(H, CROSS)
    cross[1] = w1[:, HALF:, :HALF].transpose(0, 2, 1).reshape(H, CROSS)
    w1_t = np.zeros((128, 2, 3, H), np.float32)
    for n in range(2):
        w1_t[:W_SIZES[n], :, n, :] = pairs[:, :, W_COLS[n]:W_COLS[n] + W_SIZES[n]].transpose(2, 0, 1)
        for b in range(HALF):
            w1_t[tri(b) + b, 1, n, :] = 0.0
    for t in range(3):
        part = cross[:, :, SECOND_CUTS[t]:SECOND_CUTS[t + 1]].transpose(2, 0, 1)
        w1_t[SECOND_ROW[t]:SECOND_ROW[t] + len(part), :, t, :] = part
    factors = np.ones((128, HALF + 1 + HIGH_TILES), np.float32)
    for b in range(HALF):
        factors[tri(b) + b, :HALF + 1] = 1 / 2
    for n, (row, column) in enumerate(((FIELD_PAIRS, 0), (0, HALF + 1))):
        for k in range(HALF):
            for j in range(k + 1):
                for i in range(j + 1):
                    place, at = divmod(INNER_AT[n][k] + tri(j) + i, PLACE[n])
                    factors[row + at, column + place] = 1 / (1, 2, 6)[3 - len({i, j, k})]
    arrays = {
        "x_cols": x_cols.reshape(128, GROUPS * MC),
        "w_pairs": pairs.transpose(1, 0, 2).reshape(H, -1),
        "w1_t": w1_t.reshape(128, -1),
        "w2_t": w2.transpose(1, 2, 0).reshape(H, M * H),
        "b2": b2.reshape(H, 1),
        "eye": np.eye(H, dtype=np.float32),
        "factors": factors,
    }
    arrays = {name: np.ascontiguousarray(a) for name, a in arrays.items()}
    nc = bacc.Bacc("TRN2", target_bir_lowering=False, num_devices=1)
    args = [nc.dram_tensor(name, a.shape, F32, kind="ExternalInput").ap() for name, a in arrays.items()]
    out = nc.dram_tensor("out_t", (2, H, BATCH), F32, kind="ExternalOutput").ap()
    build(nc, *args, out)
    got = run_bass_kernel_spmd(nc, [arrays], core_ids=[0]).results[0]["out_t"]
    return np.ascontiguousarray(got.transpose(2, 0, 1).reshape(BATCH, 2 * H))
```
